# Optimizing a Trainium2 kernel written in Bass

```python
import numpy as np
import jax
import jax.numpy as jnp

def _softmax(x, axis=-1):
    return jax.nn.softmax(x, axis=axis)

def _gelu(x):
    return jax.nn.gelu(x, approximate=True)

def _silu(x):
    return jax.nn.silu(x)

def _sigmoid(x):
    return jax.nn.sigmoid(x)

def _layernorm(x, axis=-1, eps=1e-05):
    m = jnp.mean(x, axis=axis, keepdims=True)
    v = jnp.var(x, axis=axis, keepdims=True)
    return (x - m) / jnp.sqrt(v + eps)

def _scatter_add(tgt, idx, src, axis=0):
    return tgt.at[idx].add(src)

def _segment_sum(src, seg, n):
    return jax.ops.segment_sum(src, seg, n)
kernel_name = 'mk_gnn_resnorm_d1_gnn_r16_9d0d69'

def setup_inputs(seed: int=0):
    np.random.seed(seed)
    _w = jnp.asarray

    def _rec_inputs():
        import jax
        import jax.numpy as jnp
        _gk = jax.random.key(seed)
        x = -0.0003713 + 1 * jax.random.normal(jax.random.fold_in(_gk, 1), (6250, 256), jnp.float32)
        src = jax.random.randint(jax.random.fold_in(_gk, 2), (100000,), 0, 6250, jnp.int32)
        dst = jax.random.randint(jax.random.fold_in(_gk, 3), (100000,), 0, 6250, jnp.int32)
        _o = jnp.argsort(dst, stable=True)
        src = src[_o]
        dst = dst[_o]
        return (x, src, dst)
    x, src, dst = _rec_inputs()

    def _L0_gnn_setup():
        import jax, jax.numpy as jnp
        import numpy as np
        N_NODES = 3125

        def _gcn_layer(h_in, W, b, src, dst, norm_edge, n_nodes):
            h = h_in @ W
            msg = h[src] * norm_edge[:, None]
            agg = jax.ops.segment_sum(msg, dst, num_segments=n_nodes)
            return agg + b
        key = jax.random.key(seed)
        ks = jax.random.split(key, 8)
        n, c_in, c_out = (N_NODES, 256, 256)
        hid = 2 * c_out
        E = 50000
        x = jax.random.normal(ks[0], (n, c_in), dtype=jnp.float32)
        edge_index = jax.random.randint(ks[1], (2, E), 0, n, dtype=jnp.int64)

        def glorot(k, fan_in, fan_out):
            s = jnp.sqrt(6.0 / (fan_in + fan_out)).astype(jnp.float32)
            return jax.random.uniform(k, (fan_in, fan_out), jnp.float32, -s, s)
        return {'x': x, 'edge_index': edge_index, 'W1': glorot(ks[2], c_in, hid), 'b1': jnp.zeros((hid,), jnp.float32), 'W2': glorot(ks[3], hid, hid), 'b2': jnp.zeros((hid,), jnp.float32), 'W3': glorot(ks[4], hid, c_out), 'b3': jnp.zeros((c_out,), jnp.float32)}
    _L0_gnn_all = _L0_gnn_setup()
    _L0_gnn_in = {k: v for k, v in _L0_gnn_all.items() if k in ('W1', 'b1', 'W2', 'b2', 'W3', 'b3')}
    del _L0_gnn_all
    return {'x': x, 'src': src, 'dst': dst, 'L0_gnn_W1': _L0_gnn_in['W1'], 'L0_gnn_b1': _L0_gnn_in['b1'], 'L0_gnn_W2': _L0_gnn_in['W2'], 'L0_gnn_b2': _L0_gnn_in['b2'], 'L0_gnn_W3': _L0_gnn_in['W3'], 'L0_gnn_b3': _L0_gnn_in['b3']}

def reference(x, src, dst, L0_gnn_W1, L0_gnn_b1, L0_gnn_W2, L0_gnn_b2, L0_gnn_W3, L0_gnn_b3):
    import jax
    import jax.numpy as jnp

    def _L0_gnn_ref(x, edge_index, W1, b1, W2, b2, W3, b3):
        import jax, jax.numpy as jnp
        import numpy as np
        N_NODES = 3125

        def _gcn_layer(h_in, W, b, src, dst, norm_edge, n_nodes):
            h = h_in @ W
            msg = h[src] * norm_edge[:, None]
            agg = jax.ops.segment_sum(msg, dst, num_segments=n_nodes)
            return agg + b
        n = x.shape[0]
        loops = jnp.arange(n, dtype=edge_index.dtype)
        src = jnp.concatenate([edge_index[0], loops])
        dst = jnp.concatenate([edge_index[1], loops])
        deg = jax.ops.segment_sum(jnp.ones_like(dst, dtype=x.dtype), dst, num_segments=n)
        dinv = jnp.where(deg > 0, jax.lax.rsqrt(deg), 0.0)
        norm_edge = dinv[src] * dinv[dst]
        h = x
        for W, b in ((W1, b1), (W2, b2), (W3, b3)):
            h = jax.nn.relu(_gcn_layer(h, W, b, src, dst, norm_edge, n))
        return h
    edge_index = jnp.stack([src, dst])
    x = _layernorm(x + _L0_gnn_ref(x, edge_index, L0_gnn_W1, L0_gnn_b1, L0_gnn_W2, L0_gnn_b2, L0_gnn_W3, L0_gnn_b3), axis=-1)
    return x

_drawn_inputs = setup_inputs


def setup_inputs(seed=0):
    import zlib

    import numpy as np

    out = dict(_drawn_inputs(seed))
    spreads = {'L0_gnn_b1': (0.0, 0.267), 'L0_gnn_b2': (0.0, 0.1), 'L0_gnn_b3': (0.0, 0.1)}
    factors = {'L0_gnn_W1': 8.0}
    for name, (base, spread) in spreads.items():
        noise = np.random.default_rng([zlib.crc32(name.encode()), seed]).standard_normal(out[name].shape)
        drawn = base * np.exp(spread * noise) if base else spread * noise
        out[name] = jnp.asarray(drawn.astype(out[name].dtype))
    for name, factor in factors.items():
        out[name] = (out[name] * factor).astype(out[name].dtype)
    return out
```

```python
from contextlib import ExitStack

import concourse.bass as bass
from concourse import mybir
from concourse.alu_op_type import AluOpType as ALU

F32 = mybir.dt.float32
BF16 = mybir.dt.bfloat16
I32 = mybir.dt.int32
ACT = mybir.ActivationFunctionType
AX = mybir.AxisListType

P = 128
SLOTS = 18
FRONT = 9
GROUPS = [range(0, 1), range(1, 3), range(3, 6), range(6, 9), range(9, 12), range(12, 15), range(15, 18)]
SURE = 16
ORDER = [*range(0, SURE - 1), *range(SURE, SLOTS), SURE - 1]
HOT_DVE = 29
HOT_ACT = 4
HOT = HOT_DVE + HOT_ACT
LAST_PLACES = [(3, 5, 9), (3, 5, 5), (5, 9, 12)]
BIG = 1 << 20
LN_EPS = 1e-5


def gnn_program(nc, x, src, dst, W1, b1, W2, b2, W3, b3, out):
    N, C = x.shape
    E = src.shape[0]
    HID = W1.shape[1]
    T = -(-N // P)
    LAST = N - (T - 1) * P
    CH = -(-E // P)
    RA = -(-CH // P)
    COLS = RA * P
    WHOLE = E // P
    REST = E - WHOLE * P
    SWEEP = -(-CH // SLOTS)
    LATE = (T - 1) * P
    KC, KH = C // P, HID // P
    WIDTH = [C, HID, C]
    HSTEPS = -(-CH // (2 * HOT))
    XG = 7
    XSTEPS = T // XG
    X_BY = [(0, 1), (0, 2), (1, 1), (0, 3), (1, 2), (0, 4), (1, 3)]
    assert len(X_BY) == XSTEPS
    assert SWEEP * SLOTS <= COLS and CH + SLOTS <= COLS and 2 * HSTEPS * HOT <= COLS
    assert XG * XSTEPS == T and 1 < REST and 0 < LAST < P

    ctx = ExitStack()
    with ctx:
        def sb(name, shape, dt=F32):
            return ctx.enter_context(nc.sbuf_tensor(name, shape, dt))

        def sem(name):
            return ctx.enter_context(nc.semaphore(name))

        table = [nc.dram_tensor(f"table{i}", (T * P, w), F32).ap() for i, w in enumerate(WIDTH)]

        raw_src = sb("raw_src", [P, RA, P], I32)
        raw_dst = sb("raw_dst", [P, RA, P], I32)
        raw_next = sb("raw_next", [P, RA, P], I32)
        srcT = sb("srcT", [P, COLS], I32)
        dstT = sb("dstT", [P, COLS], I32)
        lo = sb("lo", [P, COLS], BF16)
        hi = sb("hi", [P, COLS], BF16)
        rows = sb("rows", [P, SLOTS, HID])
        dst_f = rows[:, 0:2, :].rearrange("p a b -> p (a b)")[:, 0:COLS]
        src_f = rows[:, 2:4, :].rearrange("p a b -> p (a b)")[:, 0:COLS]
        lo_i = rows[:, 4:6, :].rearrange("p a b -> p (a b)")[:, 0:COLS].bitcast(I32)
        hi_i = rows[:, 6:8, :].rearrange("p a b -> p (a b)")[:, 0:COLS].bitcast(I32)
        steps = rows[:, 8:12, :].rearrange("p a b -> p (a b)")[:, 0:P * HOT_DVE // 2].bitcast(BF16).rearrange(
            "p (j c) -> p j c", j=P)
        viol = rows[:, 12:14, :].rearrange("p a b -> p (a b)")[:, 0:COLS]
        late_hot = rows[:, 0:3, :].rearrange("p a b -> p (a b)")[:, 0:P * SLOTS // 2].bitcast(BF16).rearrange(
            "p (k j) -> p k j", j=P)
        first_hot = rows[:, 3:6, :].rearrange("p a b -> p (a b)")[:, 0:P * SLOTS // 2].bitcast(BF16).rearrange(
            "p (k j) -> p k j", j=P)
        before = rows[:, 14, 0:(T + 1) * RA].rearrange("p (t a) -> p t a", a=RA)
        few = sb("few", [P, P], I32)
        ids = sb("ids", [P, T * P], I32)
        row_i = sb("row_i", [P, 1], I32)
        row_f = sb("row_f", [P, 1])
        ident = sb("ident", [P, P])
        ones = sb("ones", [P, P])
        zeros = sb("zeros", [P, P], BF16)
        steps_f = sb("steps_f", [P, P], BF16)
        hot_v = [sb(f"hot_v{i}", [P, P + T, HOT_DVE], BF16) for i in range(2)]
        hot_a = [sb(f"hot_a{i}", [P, HOT_ACT, P + T], BF16) for i in range(2)]
        away = sb("away", [P, 2, HOT_ACT, P + T], BF16)
        deg = sb("deg", [P, T])
        root = sb("root", [P, T])
        dinv = sb("dinv", [P, T])
        ends = sb("ends", [P, RA])
        firsts = sb("firsts", [P, T + 1])
        counts = sb("counts", [P, T + 2])
        ctl = sb("ctl", [1, T + 2])
        moved = sb("moved", [1, T])
        odd = sb("odd", [1, 2, T])
        bad = sb("bad", [1, 3])
        base_i = sb("base_i", [1, T + 1], I32)
        need_i = sb("need_i", [1, T], I32)
        slot0_i = sb("slot0_i", [1, T + 1], I32)
        general_i = sb("general_i", [1, 1], I32)
        keep = sb("keep", [P, SLOTS], I32)
        above = sb("above", [P, 2, SLOTS], I32)
        early_src = sb("early_src", [P, SLOTS], I32)
        early_dst = sb("early_dst", [P, SLOTS], I32)
        late = sb("late", [P, P])
        w1 = sb("w1", [P, KC, HID])
        w2 = sb("w2", [P, KH, HID])
        w3 = sb("w3", [P, KH, C])
        b1T = sb("b1T", [P, KH])
        b2T = sb("b2T", [P, KH])
        b3b = sb("b3b", [P, C])
        eps = sb("eps", [P, 1])
        xs = sb("xs", [P, T, C])
        idx = sb("idx", [P, SLOTS], I32)
        sel = sb("sel", [P, SLOTS, P])
        acc = sb("acc", [P, HID])
        agg = sb("agg", [P, HID])
        aggT = sb("aggT", [P, HID])
        hT = sb("hT", [P, HID])
        made = sb("made", [P, HID])
        res = sb("res", [P, C])
        y1 = sb("y1", [P, C])
        y2 = sb("y2", [P, C])
        y3 = sb("y3", [P, C])
        stats = sb("stats", [P, 6])
        mv = sb("mv", [P, 2])
        sd = sb("sd", [P, 1])
        rstd = sb("rstd", [P, 1])

        ps_acc = ctx.enter_context(nc.psum_tensor("ps_acc", [P, HID], F32))
        ps_T = ctx.enter_context(nc.psum_tensor("ps_T", [P, HID], F32))
        ps_h = ctx.enter_context(nc.psum_tensor("ps_h", [P, 512], F32))
        ps_o = ctx.enter_context(nc.psum_tensor("ps_o", [P, HID], F32))
        ps_e = [ctx.enter_context(nc.psum_tensor(f"ps_e{i}", [P, 512], F32)) for i in range(2)]
        ps_d = ctx.enter_context(nc.psum_tensor("ps_d", [P, 512], F32))
        assert KH == 4
        hidden_banks = [b[:, 0:P] for b in (ps_h, ps_d, ps_e[0], ps_e[1])]

        cleared = sem("cleared")
        dst_in = sem("dst_in")
        next_in = sem("next_in")
        src_in = sem("src_in")
        dst_float = sem("dst_float")
        src_float = sem("src_float")
        src_turned = sem("src_turned")
        src_kept = sem("src_kept")
        split_i = sem("split_i")
        split_done = sem("split_done")
        steps_done = sem("steps_done")
        away_done = sem("away_done")
        ones_done = sem("ones_done")
        weights_in = sem("weights_in")
        x_in = sem("x_in")
        iota_done = sem("iota_done")
        ident_done = sem("ident_done")
        dve = sem("dve")
        edge_turned = sem("edge_turned")
        edge_kept = sem("edge_kept")
        hot_made_v = sem("hot_made_v")
        hot_made_a = sem("hot_made_a")
        hot_used = sem("hot_used")
        deg_done = sem("deg_done")
        counts_done = sem("counts_done")
        counts_in = sem("counts_in")
        root_done = sem("root_done")
        control_done = sem("control_done")
        dinv_done = sem("dinv_done")
        late_made = sem("late_made")
        late_summed = sem("late_summed")
        x_scaled = [sem("x_scaled_v"), sem("x_scaled_a")]
        table0_out = sem("table0_out")
        pool_step = sem("pool_step")
        act_step = sem("act_step")
        dve_step = sem("dve_step")
        front_idx = sem("front_idx")
        back_idx = sem("back_idx")
        front_ready = sem("front_ready")
        back_ready = sem("back_ready")
        landed = [sem(f"landed{g}") for g in range(len(GROUPS))]
        opened = sem("opened")
        front_used = sem("front_used")
        window_done = sem("window_done")
        sum_taken = sem("sum_taken")
        own_in = sem("own_in")
        res_in = sem("res_in")
        acc_used = sem("acc_used")
        agg_ready = sem("agg_ready")
        turned = sem("turned")
        aggT_ready = sem("aggT_ready")
        h_done = sem("h_done")
        hT_ready = sem("hT_ready")
        o_done = sem("o_done")
        made_ready = sem("made_ready")
        made_free = sem("made_free")
        stored = sem("stored")
        y_step = sem("y_step")
        var_ready = sem("var_ready")
        sd_ready = sem("sd_ready")
        y_ready = sem("y_ready")
        y3_free = sem("y3_free")
        y_stored = sem("y_stored")

        block = ctx.enter_context(nc.Block())

        def nth(phase, t):
            return phase * T + t

        def nth_window(phase, t, per, w):
            return (phase * T + t) * per + w

        @block.sync
        def _(sp):
            def edge_loads(to, of, shift, edges_in):
                cut = [(RA - 1) * P * P + shift, WHOLE * P + shift]
                q = WHOLE - (RA - 1) * P
                sp.dma_start(to[:, 0:RA - 1, :],
                             of[shift:cut[0]].rearrange("(a q p) -> q a p", q=P, p=P)).then_inc(edges_in, 16)
                sp.dma_start(to[0:q, RA - 1, :],
                             of[cut[0]:cut[1]].rearrange("(q p) -> q p", p=P)).then_inc(edges_in, 16)
                sp.dma_start(to[q:q + 1, RA - 1, 0:REST - shift],
                             of[cut[1]:E].rearrange("(q p) -> q p", q=1)).then_inc(edges_in, 16)

            sp.sem_inc(made_free, 1)
            sp.sem_inc(y3_free, 1)
            sp.wait_ge(cleared, 1)
            edge_loads(raw_dst, dst, 0, dst_in)
            sp.wait_ge(cleared, 2)
            edge_loads(raw_src, src, 0, src_in)
            sp.wait_ge(cleared, 3)
            edge_loads(raw_next, dst, 1, next_in)
            sp.wait_ge(cleared, 4)
            for g in range(XSTEPS):
                lo_t, hi_t = g * XG, (g + 1) * XG
                n = hi_t - lo_t - (g == XSTEPS - 1)
                sp.dma_start(xs[:, lo_t:lo_t + n, :],
                             x[lo_t * P:(lo_t + n) * P, :].rearrange("(t p) c -> p t c", p=P)).then_inc(x_in, 16)
            sp.dma_start(xs[0:LAST, T - 1, :], x[(T - 1) * P:N, :]).then_inc(x_in, 16)
            for g in range(XSTEPS):
                by, nth_of = X_BY[g]
                sp.wait_ge(x_scaled[by], nth_of)
                sp.dma_start(table[0][g * XG * P:(g + 1) * XG * P, :].rearrange("(t p) c -> p t c", p=P),
                             xs[:, g * XG:(g + 1) * XG, :]).then_inc(table0_out, 16)

            def phases(per):
                for phase in range(3):
                    width = WIDTH[phase]
                    if phase == 0:
                        sp.wait_ge(table0_out, 16 * XSTEPS)
                    else:
                        sp.wait_ge(stored, 16 * T * phase)

                    def own_rows(t):
                        sp.wait_ge(acc_used, nth(phase, t) + 1)
                        sp.dma_start(acc[:, 0:width], table[phase][bass.ds(t * P, P), :]).then_inc(own_in, 16)

                    def store(t):
                        sp.wait_ge(made_ready, nth(phase, t) + 1)
                        w = WIDTH[phase + 1]
                        sp.dma_start(table[phase + 1][bass.ds(t * P, P), :], made[:, 0:w]).then_inc(stored, 16)
                        sp.wait_ge(stored, 16 * nth(phase, t) + 16)
                        sp.sem_inc(made_free, 1)

                    def residual(t, n):
                        if not isinstance(t, int) or t > 0:
                            sp.wait_ge(y_step, 2 * t - 1)
                        sp.dma_start(res[0:n, :], x[bass.ds(t * P, n), :]).then_inc(res_in, 16)

                    def result(t, n):
                        sp.wait_ge(y_ready, t + 1)
                        sp.dma_start(out[bass.ds(t * P, n), :], y3[0:n, :]).then_inc(y_stored, 16)
                        sp.wait_ge(y_stored, 16 * t + 16)
                        sp.sem_inc(y3_free, 1)

                    own_rows(0)
                    if phase < 2:
                        with sp.Fori(1, T) as t:
                            own_rows(t)
                            store(t - 1)
                        store(T - 1)
                    else:
                        residual(0, P)
                        with sp.Fori(1, T - 1) as t:
                            own_rows(t)
                            residual(t, P)
                            result(t - 1, P)
                        own_rows(T - 1)
                        residual(T - 1, LAST)
                        result(T - 2, P)
                        result(T - 1, LAST)
                sp.wait_ge(stored, 16 * 2 * T)
                sp.wait_ge(y_stored, 16 * T)

            sp.wait_ge(control_done, 1)
            general = sp.value_load(general_i[0:1, 0:1], min_val=0, max_val=1)
            with sp.If(general == 0):
                phases(1)
            with sp.Else():
                phases(SWEEP)

        @block.gpsimd
        def _(pool):
            nc.gpsimd.iota(few[:, :], pattern=[[1, P]], base=0, channel_multiplier=0).then_inc(iota_done, 1)
            nc.gpsimd.iota(row_i[:, :], pattern=[[0, 1]], base=0, channel_multiplier=1).then_inc(iota_done, 1)
            nc.gpsimd.iota(ids[:, :], pattern=[[1, T * P]], base=0, channel_multiplier=0).then_inc(iota_done, 1)

            def gather(phase, k, nodes=T * P):
                g = next(i for i, s in enumerate(GROUPS) if k in s)
                pool.indirect_dma_start(
                    out=rows[:, k, 0:WIDTH[phase]], out_offset=None, in_=table[phase][0:nodes, :],
                    in_offset=bass.IndirectOffsetOnAxis(ap=idx[:, k:k + 1], axis=0)).then_inc(landed[g], 16)

            def gather_if(need, phase, k, at_least):
                g = next(i for i, s in enumerate(GROUPS) if k in s)
                with pool.If(need >= at_least):
                    gather(phase, k)
                with pool.Else():
                    pool.inc_swdge_sem([landed[g]], [16])

            def window(phase, v, need, nodes=T * P):
                pool.wait_ge(front_idx, v + 1)
                pool.sem_inc(pool_step, 1)
                if need is None:
                    gather(phase, 0, nodes)
                else:
                    gather_if(need, phase, 0, SLOTS)
                for k in range(1, FRONT):
                    gather(phase, k, nodes)
                pool.wait_ge(back_idx, v + 1)
                pool.sem_inc(pool_step, 1)
                for k in range(FRONT, SLOTS):
                    if need is None or k < SURE:
                        gather(phase, k, nodes)
                    else:
                        gather_if(need, phase, k, k)

            def one_window():
                for phase in range(3):
                    if phase == 0:
                        pool.wait_ge(table0_out, 16 * XSTEPS)
                        pool.sem_inc(pool_step, 1)
                        window(phase, 0, None)
                    else:
                        pool.wait_ge(stored, 16 * (T * phase - 1))
                        pool.sem_inc(pool_step, 1)
                        window(phase, nth(phase, 0), None, LATE)
                        pool.wait_ge(stored, 16 * T * phase)
                        pool.sem_inc(pool_step, 1)
                    with pool.Fori(1, T) as t:
                        need = pool.value_load(need_i[0:1, bass.ds(t, 1)], min_val=0, max_val=99)
                        window(phase, nth(phase, t), need)

            def sweeps():
                for phase in range(3):
                    if phase == 0:
                        pool.wait_ge(table0_out, 16 * XSTEPS)
                    else:
                        pool.wait_ge(stored, 16 * T * phase)
                    pool.sem_inc(pool_step, 1)
                    with pool.Fori(0, T) as t:
                        with pool.Fori(0, SWEEP) as w:
                            window(phase, nth_window(phase, t, SWEEP, w), None)

            pool.wait_ge(control_done, 1)
            general = pool.value_load(general_i[0:1, 0:1], min_val=0, max_val=1)
            with pool.If(general == 0):
                one_window()
            with pool.Else():
                sweeps()

        @block.vector
        def _(v_):
            v = nc.vector
            done = [0]

            def step(ins):
                done[0] += 1
                ins.then_inc(dve, 1)
                v_.wait_ge(dve, done[0])

            v.memset(raw_dst[:, RA - 1, :], -1).then_inc(cleared, 1)
            v.memset(raw_src[:, RA - 1, :], 0).then_inc(cleared, 1)
            v.memset(raw_next[:, RA - 1, :], BIG).then_inc(cleared, 1)
            v.memset(xs[:, T - 1, :], 0.0).then_inc(cleared, 1)
            v.memset(ones[:, :], 1.0)
            v.memset(eps[:, :], LN_EPS)
            v.memset(zeros[:, :], 0.0).then_inc(ones_done, 1)
            v_.wait_ge(iota_done, 2)
            step(v.tensor_copy(row_f[:, :], row_i[:, :]))
            v.tensor_scalar(ident[:, :], few[:, :], row_f[:, 0:1], None, ALU.is_equal).then_inc(ident_done, 1)
            step(v.tensor_copy(steps_f[:, :], few[:, :]))
            v.tensor_copy(steps[:, :, :], steps_f[:, :].unsqueeze(2).broadcast_to([P, P, HOT_DVE])).then_inc(steps_done, 1)

            v_.wait_ge(dst_in, 16 * 3)
            v.tensor_copy(dst_f, raw_dst[:, :, :].rearrange("p a b -> p (a b)")).then_inc(dst_float, 1)
            for a in range(RA):
                v_.wait_ge(edge_turned, a + 1)
                v.tensor_copy(dstT[:, a * P:(a + 1) * P], ps_e[a % 2][:, 0:P]).then_inc(edge_kept, 1)
            v_.wait_ge(edge_kept, RA)
            v.tensor_scalar(lo_i, dstT[:, :], P - 1, None, ALU.bitwise_and).then_inc(split_i, 1)
            step(v.tensor_scalar(hi_i, dstT[:, :], P.bit_length() - 1, None, ALU.arith_shift_right))
            v.tensor_copy(hi[:, :], hi_i).then_inc(split_done, 1)
            v_.wait_ge(split_done, 2)
            v_.wait_ge(steps_done, 1)

            with v_.Fori(0, HSTEPS) as i:
                for b in range(2):
                    v_.wait_ge(hot_used, 2 * i + b + 1)
                    c0 = (2 * i + b) * HOT
                    v.tensor_tensor(hot_v[b][:, 0:P, :], steps[:, :, :],
                                    lo[:, bass.ds(c0, HOT_DVE)].unsqueeze(1).broadcast_to([P, P, HOT_DVE]), ALU.is_equal)
                    v.tensor_tensor(hot_v[b][:, P:P + T, :], steps[:, 0:T, :],
                                    hi[:, bass.ds(c0, HOT_DVE)].unsqueeze(1).broadcast_to([P, T, HOT_DVE]),
                                    ALU.is_equal).then_inc(hot_made_v, 1)

            v_.wait_ge(deg_done, 1)
            v.tensor_scalar(deg[:, :], ps_d[:, 0:T], 1.0, None, ALU.add).then_inc(deg_done, 1)
            v_.wait_ge(root_done, 1)
            v.reciprocal(dinv[:, :], root[:, :]).then_inc(dinv_done, 1)
            v_.wait_ge(dinv_done, 1)
            v_.wait_ge(x_in, 16 * (XSTEPS + 1))
            for g in range(XSTEPS):
                if X_BY[g][0] == 0:
                    t0 = g * XG
                    v.tensor_tensor(xs[:, t0:t0 + XG, :], xs[:, t0:t0 + XG, :],
                                    dinv[:, t0:t0 + XG].unsqueeze(2).broadcast_to([P, XG, C]),
                                    ALU.mult).then_inc(x_scaled[0], 1)

            v_.wait_ge(next_in, 16 * 3)
            v.tensor_scalar(firsts[:, :], few[:, 0:T + 1], float(P), None, ALU.mult)
            step(v.tensor_copy(ends[:, :], raw_next[:, :, P - 2]))
            step(v.tensor_tensor(before, ends[:, :].unsqueeze(1).broadcast_to([P, T + 1, RA]),
                                 firsts[:, :].unsqueeze(2).broadcast_to([P, T + 1, RA]), ALU.is_lt))
            step(v.tensor_reduce(counts[:, 0:T + 1], before, AX.X, ALU.add))
            step(v.tensor_tensor(viol, raw_dst[:, :, :].rearrange("p a b -> p (a b)"),
                                 raw_next[:, :, :].rearrange("p a b -> p (a b)"), ALU.is_gt))
            v.tensor_reduce(counts[:, T + 1:T + 2], viol, AX.X, ALU.add).then_inc(counts_in, 1)
            v_.wait_ge(counts_done, 1)
            step(v.tensor_copy(ctl[:, :], ps_T[0:1, 0:T + 2]))
            step(v.tensor_tensor(moved[:, :], ctl[:, 1:T + 1], ctl[:, 0:T], ALU.subtract))
            v.tensor_scalar(odd[:, 0, :], moved[:, :], float(FRONT), None, ALU.is_lt)
            step(v.tensor_scalar(odd[:, 1, :], moved[:, :], float(SLOTS - 1), None, ALU.is_gt))
            step(v.tensor_reduce(bad[:, 0:1], odd[:, :, :].rearrange("p a b -> p (a b)"), AX.X, ALU.add))
            step(v.tensor_tensor(bad[:, 1:2], bad[:, 0:1], ctl[:, T + 1:T + 2], ALU.add))
            step(v.tensor_scalar(bad[:, 2:3], bad[:, 1:2], 0.0, None, ALU.is_gt))
            v.tensor_copy(general_i[:, :], bad[:, 2:3])
            v.tensor_copy(base_i[:, :], ctl[:, 0:T + 1])
            v.tensor_copy(need_i[:, 1:T], moved[:, 1:T])
            v.memset(need_i[:, 0:1], 99)
            v.tensor_copy(slot0_i[:, 1:T + 1], moved[:, :])
            v.memset(slot0_i[:, 0:1], 0).then_inc(control_done, 1)
            v_.wait_ge(control_done, 1)

            v_.wait_ge(iota_done, 3)
            v_.wait_ge(src_kept, RA)
            v.tensor_tensor(late_hot, ids[:, LATE:LATE + P].unsqueeze(1).broadcast_to([P, SLOTS, P]),
                            srcT[:, 0:SLOTS].unsqueeze(2).broadcast_to([P, SLOTS, P]), ALU.is_equal)
            v.tensor_tensor(first_hot, few[:, :].unsqueeze(1).broadcast_to([P, SLOTS, P]),
                            dstT[:, 0:SLOTS].unsqueeze(2).broadcast_to([P, SLOTS, P]), ALU.is_equal).then_inc(late_made, 1)
            v.tensor_scalar(keep[:, :], srcT[:, 0:SLOTS], LATE, None, ALU.is_lt)
            step(v.tensor_scalar(above[:, 0, :], dstT[:, 0:SLOTS], 1, None, ALU.add))
            v.tensor_tensor(early_src[:, :], srcT[:, 0:SLOTS], keep[:, :], ALU.mult)
            step(v.tensor_tensor(above[:, 1, :], above[:, 0, :], keep[:, :], ALU.mult))
            step(v.tensor_scalar(early_dst[:, :], above[:, 1, :], 1, None, ALU.subtract))
            v_.wait_ge(late_summed, 1)
            v.tensor_copy(late[:, :], ps_d[:, 0:P])

            def prepare(n, t, base, part):
                if part == 0:
                    v_.wait_ge(front_used, n + 1)
                else:
                    v_.wait_ge(opened, n + 1)
                k = part * FRONT
                v.tensor_copy(idx[:, k:k + FRONT], srcT[:, bass.ds(base + k, FRONT)]).then_inc((front_idx, back_idx)[part], 1)
                v.tensor_tensor(sel[:, k:k + FRONT, :],
                                ids[:, bass.ds(t * P, P)].unsqueeze(1).broadcast_to([P, FRONT, P]),
                                dstT[:, bass.ds(base + k, FRONT)].unsqueeze(2).broadcast_to([P, FRONT, P]),
                                ALU.is_equal).then_inc((front_ready, back_ready)[part], 1)

            def prepare_early(n, part):
                if part == 0:
                    v_.wait_ge(front_used, n + 1)
                else:
                    v_.wait_ge(window_done, n)
                k = part * FRONT
                v.tensor_copy(idx[:, k:k + FRONT], early_src[:, k:k + FRONT]).then_inc((front_idx, back_idx)[part], 1)
                v.tensor_tensor(sel[:, k:k + FRONT, :], few[:, :].unsqueeze(1).broadcast_to([P, FRONT, P]),
                                early_dst[:, k:k + FRONT].unsqueeze(2).broadcast_to([P, FRONT, P]),
                                ALU.is_equal).then_inc((front_ready, back_ready)[part], 1)

            def take_sum(phase, n, tile, first):
                v_.wait_ge(window_done, n + 1)
                if first:
                    v_.wait_ge(own_in, 16 * (tile + 1))
                w = WIDTH[phase]
                v.tensor_tensor(acc[:, 0:w], ps_acc[:, 0:w], acc[:, 0:w], ALU.add).then_inc(sum_taken, 1)

            def finish(t, taken):
                v_.wait_ge(sum_taken, taken)
                v.scalar_tensor_tensor(y1[:, :], acc[:, 0:C], dinv[:, bass.ds(t, 1)], b3b[:, :], ALU.mult, ALU.add).then_inc(acc_used, 1)
                v_.wait_ge(acc_used, nth(2, t) + 2)
                v_.wait_ge(res_in, 16 * (t + 1))
                v.scalar_tensor_tensor(y2[:, :], y1[:, :], 0.0, res[:, :], ALU.max, ALU.add).then_inc(y_step, 1)
                v_.wait_ge(y_step, 2 * t + 1)
                v.bn_stats(stats[:, :], y2[:, :]).then_inc(y_step, 1)
                v_.wait_ge(y_step, 2 * t + 2)
                v_.sem_inc(dve_step, 1)
                v.bn_aggr(mv[:, :], stats[:, :]).then_inc(var_ready, 1)
                v_.wait_ge(sd_ready, t + 1)
                v.reciprocal(rstd[:, :], sd[:, :]).then_inc(var_ready, 1)
                v_.wait_ge(var_ready, 2 * t + 2)
                v_.wait_ge(y3_free, t + 1)
                v.tensor_scalar(y3[:, :], y2[:, :], mv[:, 0:1], rstd[:, 0:1], ALU.subtract, ALU.mult).then_inc(y_ready, 1)

            def base_of(t):
                return v_.value_load(base_i[0:1, bass.ds(t, 1)], min_val=0, max_val=CH - 1)

            def one_window():
                prepare(0, 0, 0, 0)
                prepare(0, 0, 0, 1)
                for phase in range(3):
                    with v_.Fori(1, T) as t:
                        n = nth(phase, t)
                        base = base_of(t)
                        prepare(n, t, base, 0)
                        take_sum(phase, n - 1, n - 1, True)
                        prepare(n, t, base, 1)
                        if phase == 2:
                            finish(t - 1, n + 1)
                    n = nth(phase, T)
                    if phase < 2:
                        prepare_early(n, 0)
                    take_sum(phase, n - 1, n - 1, True)
                    if phase < 2:
                        prepare_early(n, 1)
                    if phase == 2:
                        finish(T - 1, n + 1)

            def sweeps():
                for phase in range(3):
                    with v_.Fori(0, T) as t:
                        tile = nth(phase, t)

                        def one(w, first):
                            n = nth_window(phase, t, SWEEP, w)
                            prepare(n, t, w * SLOTS, 0)
                            prepare(n, t, w * SLOTS, 1)
                            v_.wait_ge(sum_taken, n + 1)
                            take_sum(phase, n, tile, first)
                        one(0, True)
                        with v_.Fori(1, SWEEP) as w:
                            one(w, False)
                        if phase == 2:
                            finish(t, (tile + 1) * SWEEP + 1)

            general = v_.value_load(general_i[0:1, 0:1], min_val=0, max_val=1)
            with v_.If(general == 0):
                one_window()
            with v_.Else():
                sweeps()

        @block.scalar
        def _(act):
            act.wait_ge(src_in, 16 * 3)
            nc.scalar.activation(src_f, raw_src[:, :, :].rearrange("p a b -> p (a b)"), ACT.Copy).then_inc(src_float, 1)
            act.wait_ge(split_i, 1)
            nc.scalar.activation(lo[:, :], lo_i, ACT.Copy).then_inc(split_done, 1)
            act.wait_ge(next_in, 16 * 3)
            act.dma_start(w1[:, :, :], W1.rearrange("(k p) n -> p k n", p=P)).then_inc(weights_in, 16)
            act.dma_start(w2[:, :, :], W2.rearrange("(k p) n -> p k n", p=P)).then_inc(weights_in, 16)
            act.dma_start(w3[:, :, :], W3.rearrange("(k p) n -> p k n", p=P)).then_inc(weights_in, 16)
            act.dma_start(b3b[:, :], b3.rearrange("(a c) -> a c", a=1).broadcast_to([P, C])).then_inc(weights_in, 16)
            with nc.allow_non_contiguous_dma(reason="two bias vectors, one value to a partition"):
                act.dma_start(b1T[:, :], b1.rearrange("(m p) -> p m", p=P)).then_inc(weights_in, 16)
                act.dma_start(b2T[:, :], b2.rearrange("(m p) -> p m", p=P)).then_inc(weights_in, 16)

            act.wait_ge(split_done, 2)
            act.wait_ge(steps_done, 1)
            with act.Fori(0, HSTEPS) as i:
                for b in range(2):
                    act.wait_ge(hot_used, 2 * i + b + 1)
                    act.sem_inc(act_step, 1)
                    c0 = (2 * i + b) * HOT + HOT_DVE
                    for c in range(HOT_ACT):
                        nc.scalar.activation(away[:, b, c, 0:P], steps_f[:, :], ACT.Abs, bias=lo[:, bass.ds(c0 + c, 1)], scale=-1.0)
                        last = nc.scalar.activation(away[:, b, c, P:P + T], steps_f[:, 0:T], ACT.Abs,
                                                    bias=hi[:, bass.ds(c0 + c, 1)], scale=-1.0)
                    last.then_inc(away_done, 1)
                    act.wait_ge(away_done, 2 * i + b + 1)
                    nc.scalar.activation(hot_a[b][:, :, :], away[:, b, :, :], ACT.Relu, bias=ones[:, 0:1],
                                         scale=-1.0).then_inc(hot_made_a, 1)
            act.wait_ge(deg_done, 2)
            nc.scalar.activation(root[:, :], deg[:, :], ACT.Sqrt).then_inc(root_done, 1)
            act.wait_ge(dinv_done, 1)
            act.wait_ge(x_in, 16 * (XSTEPS + 1))
            for g in range(XSTEPS):
                if X_BY[g][0] == 1:
                    for t in range(g * XG, (g + 1) * XG):
                        ins = nc.scalar.activation(xs[:, t, :], xs[:, t, :], ACT.Copy, scale=dinv[:, t:t + 1])
                    ins.then_inc(x_scaled[1], 1)
            for a in range(RA):
                act.wait_ge(src_turned, a + 1)
                nc.scalar.activation(srcT[:, a * P:(a + 1) * P], ps_e[a % 2][:, 0:P], ACT.Copy).then_inc(src_kept, 1)
            act.sem_inc(acc_used, 1)
            act.wait_ge(weights_in, 16 * 6)

            def scale(phase, t, per):
                n = nth(phase, t)
                w = WIDTH[phase]
                act.wait_ge(sum_taken, (n + 1) * per + 1)
                act.sem_inc(act_step, 1)
                nc.scalar.activation(agg[:, 0:w], acc[:, 0:w], ACT.Copy, scale=dinv[:, bass.ds(t, 1)]).then_inc(agg_ready, 1)
                act.wait_ge(agg_ready, n + 1)
                act.sem_inc(acc_used, 1)

            def relu_T(ps, bias, m):
                nc.scalar.activation(hT[:, m * P:(m + 1) * P], ps, ACT.Relu,
                                     bias=bias[:, m:m + 1]).then_inc(hT_ready, 1)

            def tile(phase, t, per):
                n = nth(phase, t)
                scale(phase, t, per)
                if phase == 0:
                    act.wait_ge(turned, n + 1)
                    nc.scalar.activation(aggT[:, 0:C], ps_T[:, 0:C], ACT.Copy).then_inc(aggT_ready, 1)
                    for m in range(KH):
                        act.wait_ge(h_done, KH * t + m + 1)
                        relu_T(hidden_banks[m], b1T, m)
                else:
                    act.wait_ge(turned, n + 1)
                    for m in range(KH):
                        relu_T(ps_T[:, m * P:(m + 1) * P], b2T, m)
                w = WIDTH[phase + 1]
                act.wait_ge(o_done, n + 1)
                act.wait_ge(made_free, n + 1)
                act.sem_inc(act_step, 1)
                nc.scalar.activation(made[:, 0:w], ps_o[:, 0:w], ACT.Copy, scale=dinv[:, bass.ds(t, 1)]).then_inc(made_ready, 1)

            def deviation(t):
                act.wait_ge(var_ready, 2 * t + 1)
                nc.scalar.activation(sd[:, :], mv[:, 1:2], ACT.Sqrt, bias=eps[:, 0:1]).then_inc(sd_ready, 1)

            def phases(per):
                for phase in range(2):
                    with act.Fori(0, T) as t:
                        tile(phase, t, per)
                with act.Fori(0, T) as t:
                    deviation(t)

            act.wait_ge(control_done, 1)
            general = act.value_load(general_i[0:1, 0:1], min_val=0, max_val=1)
            with act.If(general == 0):
                phases(1)
            with act.Else():
                phases(SWEEP)

        @block.tensor
        def _(pe):
            mm = nc.tensor.matmul
            pe.sem_inc(hot_used, 2)
            pe.sem_inc(front_used, 1)
            pe.sem_inc(sum_taken, 1)
            pe.wait_ge(ident_done, 1)

            def turn_edges(of, floated, turned_, kept):
                pe.wait_ge(floated, 1)
                for a in range(RA):
                    if a >= 2:
                        pe.wait_ge(kept, a - 1)
                    nc.tensor.transpose(ps_e[a % 2][:, 0:P], of[:, a * P:(a + 1) * P], ident[:, :]).then_inc(turned_, 1)

            turn_edges(dst_f, dst_float, edge_turned, edge_kept)
            pe.wait_ge(ones_done, 1)
            mm(ps_d[:, 0:T], zeros[:, :], zeros[:, 0:T], start=True, stop=False, skip_group_check=True)
            with pe.Fori(0, HSTEPS) as i:
                for b in range(2):
                    n = 2 * i + b + 1

                    def add(place, tile):
                        return mm(ps_d[:, 0:T], place, tile, start=False, stop=False, skip_group_check=True)

                    pe.wait_ge(hot_made_v, n)
                    for c in range(HOT_DVE):
                        add(hot_v[b][:, 0:P, c], hot_v[b][:, P:P + T, c])
                    pe.wait_ge(hot_made_a, n)
                    for c in range(HOT_ACT):
                        last = add(hot_a[b][:, c, 0:P], hot_a[b][:, c, P:P + T])
                    last.then_inc(hot_used, 1)
            mm(ps_d[:, 0:T], zeros[:, :], zeros[:, 0:T], start=False, stop=True, skip_group_check=True).then_inc(deg_done, 1)
            pe.wait_ge(edge_kept, RA)
            turn_edges(src_f, src_float, src_turned, src_kept)
            pe.wait_ge(counts_in, 1)
            mm(ps_T[:, 0:T + 2], ones[:, :], counts[:, :], start=True, stop=True).then_inc(counts_done, 1)
            pe.wait_ge(late_made, 1)
            for k in range(SLOTS):
                ins = mm(ps_d[:, 0:P], late_hot[:, k, :], first_hot[:, k, :], start=(k == 0), stop=(k == SLOTS - 1))
            ins.then_inc(late_summed, 1)
            pe.wait_ge(control_done, 1)
            pe.wait_ge(weights_in, 16 * 6)

            def slots(phase, n, ks, first, need=None):
                w = WIDTH[phase]
                for k in ks:
                    for g, s in enumerate(GROUPS):
                        if k == next(o for o in ORDER if o in s):
                            pe.wait_ge(landed[g], 16 * len(s) * (n + 1))
                    if k == 0:
                        pe.wait_ge(front_ready, n + 1)
                        pe.wait_ge(sum_taken, n + 1)
                    if k == FRONT:
                        pe.wait_ge(back_ready, n + 1)
                    if need is not None and k >= SURE:
                        with pe.If(need >= k):
                            mm(ps_acc[:, 0:w], sel[:, k, :], rows[:, k, 0:w], start=False, stop=False)
                        continue
                    ins = mm(ps_acc[:, 0:w], sel[:, k, :], first if k == 0 else rows[:, k, 0:w],
                             start=(k == 0), stop=(k == ORDER[-1]))
                    if k == 0:
                        ins.then_inc(opened, 1)
                    if k == FRONT - 1:
                        ins.then_inc(front_used, 1)
                    if k == ORDER[-1]:
                        ins.then_inc(window_done, 1)

            def turn(phase, t):
                n = nth(phase, t)
                pe.wait_ge(agg_ready, n + 1)
                for m in range(WIDTH[phase] // P):
                    ins = nc.tensor.transpose(ps_T[:, m * P:(m + 1) * P], agg[:, m * P:(m + 1) * P], ident[:, :])
                ins.then_inc(turned, 1)

            def hidden(t):
                pe.wait_ge(aggT_ready, t + 1)
                for m in range(KH):
                    for k in range(KC):
                        ins = mm(hidden_banks[m], w1[:, k, m * P:(m + 1) * P], aggT[:, k * P:(k + 1) * P],
                                 start=(k == 0), stop=(k == KC - 1))
                    ins.then_inc(h_done, 1)

            def product(phase, t):
                n = nth(phase, t)
                w = WIDTH[phase + 1]
                wt = w2 if phase == 0 else w3
                for m in range(KH):
                    pe.wait_ge(hT_ready, KH * n + m + 1)
                    ins = mm(ps_o[:, 0:w], hT[:, m * P:(m + 1) * P], wt[:, m, :], start=(m == 0), stop=(m == KH - 1))
                ins.then_inc(o_done, 1)

            def one_window():
                for phase in range(3):
                    def first_rows(t):
                        at = pe.value_load(slot0_i[0:1, bass.ds(t, 1)], min_val=0, max_val=SLOTS - 1)
                        return rows[:, bass.ds(at, 1), 0:WIDTH[phase]].rearrange("p a w -> p (a w)")

                    def steady(t, places):
                        n = nth(phase, t)
                        need = pe.value_load(need_i[0:1, bass.ds(t, 1)], min_val=0, max_val=99)
                        at_turn, at_hidden, at_product = places
                        slots(phase, n, ORDER[0:at_turn], first_rows(t))
                        if phase < 2:
                            turn(phase, t - 1)
                        slots(phase, n, ORDER[at_turn:at_hidden], None, need)
                        if phase == 0:
                            hidden(t - 1)
                        slots(phase, n, ORDER[at_hidden:at_product], None, need)
                        if phase < 2:
                            product(phase, t - 1)
                        slots(phase, n, ORDER[at_product:], None, need)

                    n = nth(phase, 0)
                    slots(phase, n, ORDER[:-1], rows[:, 0, 0:WIDTH[phase]])
                    if phase > 0:
                        pe.wait_ge(made_ready, n)
                        mm(ps_acc[:, 0:WIDTH[phase]], late[:, :], made[:, 0:WIDTH[phase]], start=False, stop=False)
                    slots(phase, n, ORDER[-1:], None)
                    with pe.Fori(1, T - 1) as t:
                        steady(t, (5, 9, SLOTS if phase == 1 else 12))
                    steady(T - 1, LAST_PLACES[phase])
                    if phase < 2:
                        turn(phase, T - 1)
                        if phase == 0:
                            hidden(T - 1)
                        product(phase, T - 1)

            def sweeps():
                for phase in range(3):
                    with pe.Fori(0, T) as t:
                        with pe.Fori(0, SWEEP) as w:
                            slots(phase, nth_window(phase, t, SWEEP, w), ORDER, rows[:, 0, 0:WIDTH[phase]])
                        if phase < 2:
                            turn(phase, t)
                            if phase == 0:
                                hidden(t)
                            product(phase, t)

            general = pe.value_load(general_i[0:1, 0:1], min_val=0, max_val=1)
            with pe.If(general == 0):
                one_window()
            with pe.Else():
                sweeps()


_INS = ['x', 'src', 'dst', 'L0_gnn_W1', 'L0_gnn_b1', 'L0_gnn_W2', 'L0_gnn_b2', 'L0_gnn_W3', 'L0_gnn_b3']


def kernel(**inputs):
    import numpy as _np
    import concourse.bacc as _bacc
    from concourse import mybir as _mybir
    from concourse.bass_utils import run_bass_kernel_spmd as _run

    nc = _bacc.Bacc("TRN2", target_bir_lowering=False, num_devices=1)
    arrays, args = {}, []
    for name in _INS:
        a = _np.ascontiguousarray(inputs[name])
        arrays[f"in_{name}_dram"] = a
        args.append(nc.dram_tensor(f"in_{name}_dram", a.shape, _mybir.dt.from_np(a.dtype), kind="ExternalInput").ap())
    out = nc.dram_tensor("out_0_dram", inputs["x"].shape, _mybir.dt.float32, kind="ExternalOutput").ap()
    gnn_program(nc, *args, out)
    r = _run(nc, [arrays], core_ids=[0])
    return r.results[0]["out_0_dram"]
```

```python
from contextlib import ExitStack

import concourse.bass as bass
from concourse import mybir
from concourse.alu_op_type import AluOpType as ALU

F32 = mybir.dt.float32
BF16 = mybir.dt.bfloat16
I32 = mybir.dt.int32
ACT = mybir.ActivationFunctionType
AX = mybir.AxisListType

P = 128
SLOTS = 18
FRONT = 9
GROUPS = [range(0, 1), range(1, 3), range(3, 6), range(6, 9), range(9, 12), range(12, 15), range(15, 18)]
SURE = 16
ORDER = [*range(0, SURE - 1), *range(SURE, SLOTS), SURE - 1]
HOT_DVE = 32
HOT_ACT = 4
HALF = 64
HOT = HOT_DVE + HOT_ACT
LAST_PLACES = [(1, 2, 4), (3, 5, 5), (5, 9, 12)]
BIG = 1 << 20
LN_EPS = 1e-5


def gnn_program(nc, x, src, dst, W1, b1, W2, b2, W3, b3, out):
    N, C = x.shape
    E = src.shape[0]
    HID = W1.shape[1]
    T = -(-N // P)
    LAST = N - (T - 1) * P
    CH = -(-E // P)
    RA = -(-CH // P)
    COLS = RA * P
    WHOLE = E // P
    REST = E - WHOLE * P
    SWEEP = -(-CH // SLOTS)
    HALVES = 2 * T
    LATE = (T - 1) * P
    KC, KH = C // P, HID // P
    WIDTH = [C, HID, C]
    HSTEPS = -(-CH // (2 * HOT))
    XG = 7
    XSTEPS = T // XG
    X_BY = [(0, 1), (0, 2), (1, 1), (0, 3), (1, 2), (0, 4), (1, 3)]
    assert len(X_BY) == XSTEPS
    assert SWEEP * SLOTS <= COLS and CH + SLOTS <= COLS and 2 * HSTEPS * HOT <= COLS
    assert XG * XSTEPS == T and 1 < REST and 0 < LAST < P
    assert SLOTS * P <= WHOLE * P and C + 2 * P <= HID and HALVES <= P and FRONT * T <= 512

    ctx = ExitStack()
    with ctx:
        def sb(name, shape, dt=F32):
            return ctx.enter_context(nc.sbuf_tensor(name, shape, dt))

        def sem(name):
            return ctx.enter_context(nc.semaphore(name))

        table = [nc.dram_tensor(f"table{i}", (T * P, w), F32).ap() for i, w in enumerate(WIDTH)]

        places = nc.dram_tensor("places", (SLOTS, P), I32).ap()

        raw_src = sb("raw_src", [P, RA, P], I32)
        raw_dst = sb("raw_dst", [P, RA, P], I32)
        raw_next = sb("raw_next", [P, RA, P], I32)
        srcT = sb("srcT", [P, COLS], I32)
        dstT = sb("dstT", [P, COLS], I32)
        lo = sb("lo", [P, COLS], BF16)
        hi = sb("hi", [P, COLS], BF16)
        rows = sb("rows", [P, SLOTS, HID])
        src_f = sb("src_f", [P, COLS])[:, :]
        sel = sb("sel", [P, SLOTS, P])
        src_wide = rows[:, :, C:C + P].bitcast(I32)
        is_here = rows[:, :, C + P:C + 2 * P]
        steps = sel[:, :, :].rearrange("p a b -> p (a b)")[:, 0:HALVES * HOT_DVE // 2].bitcast(BF16).rearrange(
            "p (j c) -> p j c", j=HALVES)
        work = [sb(f"work{i}", [P, (HALF + HALVES) * HOT_DVE // 2]) for i in range(2)]
        hot_v = [w[:, :].bitcast(BF16)[:, :].rearrange("p (j c) -> p j c", c=HOT_DVE) for w in work]
        dst_f = work[0][:, 0:COLS]
        lo_i = work[0][:, COLS:2 * COLS].bitcast(I32)
        hi_i = work[1][:, 0:COLS].bitcast(I32)
        viol = work[0][:, 0:COLS]
        before = work[0][:, COLS:COLS + (T + 1) * RA].rearrange("p (t a) -> p t a", a=RA)
        in_tile = work[1][:, 0:SLOTS * T].rearrange("p (k t) -> p k t", t=T)
        of_tile = work[1][:, SLOTS * T:2 * SLOTS * T].rearrange("p (k t) -> p k t", t=T)
        late_hot = work[1][:, 0:P * SLOTS // 2].bitcast(BF16).rearrange(
            "p (k j) -> p k j", j=P)
        first_hot = work[0][:, 0:P * SLOTS // 2].bitcast(BF16).rearrange(
            "p (k j) -> p k j", j=P)
        few = sb("few", [P, P], I32)
        ids = sb("ids", [P, T * P], I32)
        row_i = sb("row_i", [P, 1], I32)
        row_f = sb("row_f", [P, 1])
        ident = sb("ident", [P, P])
        upper = sb("upper", [HALF, P])
        ones = sb("ones", [P, P])
        zeros = sb("zeros", [P, P], BF16)
        steps_f = sb("steps_f", [P, P], BF16)
        hot_a = [sb(f"hot_a{i}", [P, HOT_ACT, HALF + HALVES], BF16) for i in range(2)]
        away = sb("away", [P, 2, HOT_ACT, HALF + HALVES], BF16)
        deg = sb("deg", [HALF, 2, T])
        root = sb("root", [P, T])
        dinv = sb("dinv", [P, T])
        place = sb("place", [SLOTS, P], I32)
        tile_i = sb("tile_i", [P, SLOTS], I32)
        src_dinv = sb("src_dinv", [P, SLOTS])
        ends = sb("ends", [P, RA])
        firsts = sb("firsts", [P, T + 1])
        counts = sb("counts", [P, T + 2])
        ctl = sb("ctl", [1, T + 2])
        moved = sb("moved", [1, T])
        odd = sb("odd", [1, 2, T])
        bad = sb("bad", [1, 3])
        base_i = sb("base_i", [1, T + 1], I32)
        need_i = sb("need_i", [1, T], I32)
        slot0_i = sb("slot0_i", [1, T + 1], I32)
        general_i = sb("general_i", [1, 1], I32)
        keep = sb("keep", [P, SLOTS], I32)
        above = sb("above", [P, 2, SLOTS], I32)
        early_src = sb("early_src", [P, SLOTS], I32)
        early_dst = sb("early_dst", [P, SLOTS], I32)
        late = sb("late", [P, P])
        w1 = sb("w1", [P, KC, HID])
        w2 = sb("w2", [P, KH, HID])
        w3 = sb("w3", [P, KH, C])
        b1T = sb("b1T", [P, KH])
        b2T = sb("b2T", [P, KH])
        b3b = sb("b3b", [P, C])
        eps = sb("eps", [P, 1])
        xs = sb("xs", [P, T, C])
        idx = sb("idx", [P, SLOTS], I32)
        acc = sb("acc", [P, HID])
        agg = sb("agg", [P, HID])
        aggT = sb("aggT", [P, HID])
        hT = sb("hT", [P, HID])
        made = sb("made", [P, HID])
        res = sb("res", [P, C])
        y1 = sb("y1", [P, C])
        y2 = sb("y2", [P, C])
        y3 = sb("y3", [P, C])
        stats = sb("stats", [P, 6])
        mv = sb("mv", [P, 2])
        sd = sb("sd", [P, 1])
        rstd = sb("rstd", [P, 1])

        ps_acc = ctx.enter_context(nc.psum_tensor("ps_acc", [P, HID], F32))
        ps_T = ctx.enter_context(nc.psum_tensor("ps_T", [P, HID], F32))
        ps_h = ctx.enter_context(nc.psum_tensor("ps_h", [P, 512], F32))
        ps_o = ctx.enter_context(nc.psum_tensor("ps_o", [P, HID], F32))
        ps_e = [ctx.enter_context(nc.psum_tensor(f"ps_e{i}", [P, 512], F32)) for i in range(2)]
        ps_d = ctx.enter_context(nc.psum_tensor("ps_d", [P, 512], F32))
        ps_l = ctx.enter_context(nc.psum_tensor("ps_l", [P, 512], F32))
        assert KH == 4
        hidden_banks = [b[:, 0:P] for b in (ps_h, ps_d, ps_e[0], ps_e[1])]

        cleared = sem("cleared")
        dst_in = sem("dst_in")
        next_in = sem("next_in")
        src_in = sem("src_in")
        dst_float = sem("dst_float")
        src_float = sem("src_float")
        src_turned = sem("src_turned")
        src_kept = sem("src_kept")
        split_i = sem("split_i")
        split_done = sem("split_done")
        steps_done = sem("steps_done")
        away_done = sem("away_done")
        ones_done = sem("ones_done")
        weights_in = sem("weights_in")
        x_in = sem("x_in")
        iota_done = sem("iota_done")
        ident_done = sem("ident_done")
        dve = sem("dve")
        edge_turned = sem("edge_turned")
        edge_kept = sem("edge_kept")
        hot_made_v = sem("hot_made_v")
        hot_made_a = sem("hot_made_a")
        hot_used = sem("hot_used")
        deg_done = sem("deg_done")
        counts_done = sem("counts_done")
        counts_in = sem("counts_in")
        root_done = sem("root_done")
        control_done = sem("control_done")
        dinv_done = sem("dinv_done")
        wide_in = sem("wide_in")
        place_done = sem("place_done")
        place_out = sem("place_out")
        here_done = sem("here_done")
        src_dinv_spread = sem("src_dinv_spread")
        src_dinv_done = sem("src_dinv_done")
        front_scaled = sem("front_scaled")
        back_scaled = sem("back_scaled")
        late_made = sem("late_made")
        late_summed = sem("late_summed")
        x_scaled = [sem("x_scaled_v"), sem("x_scaled_a")]
        table0_out = sem("table0_out")
        pool_step = sem("pool_step")
        act_step = sem("act_step")
        dve_step = sem("dve_step")
        front_idx = sem("front_idx")
        back_idx = sem("back_idx")
        front_ready = sem("front_ready")
        back_ready = sem("back_ready")
        landed = [sem(f"landed{g}") for g in range(len(GROUPS))]
        opened = sem("opened")
        front_used = sem("front_used")
        window_done = sem("window_done")
        sum_taken = sem("sum_taken")
        own_in = sem("own_in")
        res_in = sem("res_in")
        acc_used = sem("acc_used")
        agg_ready = sem("agg_ready")
        turned = sem("turned")
        aggT_ready = sem("aggT_ready")
        h_done = sem("h_done")
        hT_ready = sem("hT_ready")
        o_done = sem("o_done")
        made_ready = sem("made_ready")
        made_free = sem("made_free")
        stored = sem("stored")
        y_step = sem("y_step")
        var_ready = sem("var_ready")
        sd_ready = sem("sd_ready")
        y_ready = sem("y_ready")
        y3_free = sem("y3_free")
        y_stored = sem("y_stored")

        block = ctx.enter_context(nc.Block())

        def nth(phase, t):
            return phase * T + t

        def nth_window(phase, t, per, w):
            return (phase * T + t) * per + w

        @block.sync
        def _(sp):
            def edge_loads(to, of, shift, edges_in):
                cut = [(RA - 1) * P * P + shift, WHOLE * P + shift]
                q = WHOLE - (RA - 1) * P
                sp.dma_start(to[:, 0:RA - 1, :],
                             of[shift:cut[0]].rearrange("(a q p) -> q a p", q=P, p=P)).then_inc(edges_in, 16)
                sp.dma_start(to[0:q, RA - 1, :],
                             of[cut[0]:cut[1]].rearrange("(q p) -> q p", p=P)).then_inc(edges_in, 16)
                sp.dma_start(to[q:q + 1, RA - 1, 0:REST - shift],
                             of[cut[1]:E].rearrange("(q p) -> q p", q=1)).then_inc(edges_in, 16)

            sp.sem_inc(made_free, 1)
            sp.sem_inc(y3_free, 1)
            sp.wait_ge(cleared, 1)
            edge_loads(raw_dst, dst, 0, dst_in)
            sp.wait_ge(cleared, 2)
            edge_loads(raw_src, src, 0, src_in)
            sp.wait_ge(cleared, 3)
            edge_loads(raw_next, dst, 1, next_in)
            sp.wait_ge(cleared, 4)
            for g in range(XSTEPS):
                lo_t, hi_t = g * XG, (g + 1) * XG
                n = hi_t - lo_t - (g == XSTEPS - 1)
                sp.dma_start(xs[:, lo_t:lo_t + n, :],
                             x[lo_t * P:(lo_t + n) * P, :].rearrange("(t p) c -> p t c", p=P)).then_inc(x_in, 16)
            sp.dma_start(xs[0:LAST, T - 1, :], x[(T - 1) * P:N, :]).then_inc(x_in, 16)
            sp.wait_ge(place_done, 1)
            sp.dma_start(places[:, :], place[:, :]).then_inc(place_out, 16)
            sp.wait_ge(place_out, 16)
            sp.dma_start(src_wide, places.rearrange("(a k) p -> a k p", a=1).broadcast_to([P, SLOTS, P])).then_inc(wide_in, 16)
            for g in range(XSTEPS):
                by, nth_of = X_BY[g]
                sp.wait_ge(x_scaled[by], nth_of)
                sp.dma_start(table[0][g * XG * P:(g + 1) * XG * P, :].rearrange("(t p) c -> p t c", p=P),
                             xs[:, g * XG:(g + 1) * XG, :]).then_inc(table0_out, 16)

            def phases(per):
                for phase in range(3):
                    width = WIDTH[phase]
                    if phase == 0:
                        sp.wait_ge(table0_out, 16 * XSTEPS)
                    else:
                        sp.wait_ge(stored, 16 * T * phase)

                    def own_rows(t):
                        sp.wait_ge(acc_used, nth(phase, t) + 1)
                        sp.dma_start(acc[:, 0:width], table[phase][bass.ds(t * P, P), :]).then_inc(own_in, 16)

                    def store(t):
                        sp.wait_ge(made_ready, nth(phase, t) + 1)
                        w = WIDTH[phase + 1]
                        sp.dma_start(table[phase + 1][bass.ds(t * P, P), :], made[:, 0:w]).then_inc(stored, 16)
                        sp.wait_ge(stored, 16 * nth(phase, t) + 16)
                        sp.sem_inc(made_free, 1)

                    def residual(t, n):
                        if not isinstance(t, int) or t > 0:
                            sp.wait_ge(y_step, 2 * t - 1)
                        sp.dma_start(res[0:n, :], x[bass.ds(t * P, n), :]).then_inc(res_in, 16)

                    def result(t, n):
                        sp.wait_ge(y_ready, t + 1)
                        sp.dma_start(out[bass.ds(t * P, n), :], y3[0:n, :]).then_inc(y_stored, 16)
                        sp.wait_ge(y_stored, 16 * t + 16)
                        sp.sem_inc(y3_free, 1)

                    own_rows(0)
                    if phase < 2:
                        with sp.Fori(1, T) as t:
                            own_rows(t)
                            store(t - 1)
                        store(T - 1)
                    else:
                        residual(0, P)
                        with sp.Fori(1, T - 1) as t:
                            own_rows(t)
                            residual(t, P)
                            result(t - 1, P)
                        own_rows(T - 1)
                        residual(T - 1, LAST)
                        result(T - 2, P)
                        result(T - 1, LAST)
                sp.wait_ge(stored, 16 * 2 * T)
                sp.wait_ge(y_stored, 16 * T)

            sp.wait_ge(control_done, 1)
            general = sp.value_load(general_i[0:1, 0:1], min_val=0, max_val=1)
            with sp.If(general == 0):
                phases(1)
            with sp.Else():
                phases(SWEEP)

        @block.gpsimd
        def _(pool):
            nc.gpsimd.iota(few[:, :], pattern=[[1, P]], base=0, channel_multiplier=0).then_inc(iota_done, 1)
            nc.gpsimd.iota(row_i[:, :], pattern=[[0, 1]], base=0, channel_multiplier=1).then_inc(iota_done, 1)

            pool.wait_ge(src_kept, 1)
            for k in range(SLOTS):
                g = next(i for i, s in enumerate(GROUPS) if k in s)
                pool.indirect_dma_start(
                    out=rows[:, k, 0:C], out_offset=None, in_=x[:, :],
                    in_offset=bass.IndirectOffsetOnAxis(ap=srcT[:, k:k + 1], axis=0)).then_inc(landed[g], 16)
            nc.gpsimd.iota(ids[:, :], pattern=[[1, T * P]], base=0, channel_multiplier=0).then_inc(iota_done, 1)
            pool.wait_ge(wide_in, 16)
            pool.wait_ge(ident_done, 1)
            nc.gpsimd.tensor_scalar(is_here, src_wide, row_f[:, 0:1], None, ALU.is_equal).then_inc(here_done, 1)

            def gather(phase, k, nodes=T * P):
                g = next(i for i, s in enumerate(GROUPS) if k in s)
                pool.indirect_dma_start(
                    out=rows[:, k, 0:WIDTH[phase]], out_offset=None, in_=table[phase][0:nodes, :],
                    in_offset=bass.IndirectOffsetOnAxis(ap=idx[:, k:k + 1], axis=0)).then_inc(landed[g], 16)

            def gather_if(need, phase, k, at_least):
                g = next(i for i, s in enumerate(GROUPS) if k in s)
                with pool.If(need >= at_least):
                    gather(phase, k)
                with pool.Else():
                    pool.inc_swdge_sem([landed[g]], [16])

            def window(phase, v, need, nodes=T * P):
                pool.wait_ge(front_idx, v + 1)
                pool.sem_inc(pool_step, 1)
                if need is None:
                    gather(phase, 0, nodes)
                else:
                    gather_if(need, phase, 0, SLOTS)
                for k in range(1, FRONT):
                    gather(phase, k, nodes)
                pool.wait_ge(back_idx, v + 1)
                pool.sem_inc(pool_step, 1)
                for k in range(FRONT, SLOTS):
                    if need is None or k < SURE:
                        gather(phase, k, nodes)
                    else:
                        gather_if(need, phase, k, k)

            def one_window():
                for phase in range(3):
                    if phase == 0:
                        pool.wait_ge(table0_out, 16 * XSTEPS)
                        pool.sem_inc(pool_step, 1)
                    else:
                        pool.wait_ge(stored, 16 * (T * phase - 1))
                        pool.sem_inc(pool_step, 1)
                        window(phase, nth(phase, 0), None, LATE)
                        pool.wait_ge(stored, 16 * T * phase)
                        pool.sem_inc(pool_step, 1)
                    with pool.Fori(1, T) as t:
                        need = pool.value_load(need_i[0:1, bass.ds(t, 1)], min_val=0, max_val=99)
                        window(phase, nth(phase, t), need)

            def sweeps():
                for phase in range(3):
                    if phase == 0:
                        pool.wait_ge(table0_out, 16 * XSTEPS)
                    else:
                        pool.wait_ge(stored, 16 * T * phase)
                    pool.sem_inc(pool_step, 1)
                    if phase == 0:
                        with pool.Fori(1, SWEEP) as w:
                            window(phase, w, None)
                    with pool.Fori(1 if phase == 0 else 0, T) as t:
                        with pool.Fori(0, SWEEP) as w:
                            window(phase, nth_window(phase, t, SWEEP, w), None)

            pool.wait_ge(control_done, 1)
            general = pool.value_load(general_i[0:1, 0:1], min_val=0, max_val=1)
            with pool.If(general == 0):
                one_window()
            with pool.Else():
                sweeps()

        @block.vector
        def _(v_):
            v = nc.vector
            done = [0]

            def step(ins):
                done[0] += 1
                ins.then_inc(dve, 1)
                v_.wait_ge(dve, done[0])

            v.memset(raw_dst[:, RA - 1, :], -1).then_inc(cleared, 1)
            v.memset(raw_src[:, RA - 1, :], 0).then_inc(cleared, 1)
            v.memset(raw_next[:, RA - 1, :], BIG).then_inc(cleared, 1)
            v.memset(xs[:, T - 1, :], 0.0).then_inc(cleared, 1)
            v.memset(ones[:, :], 1.0)
            v.memset(eps[:, :], LN_EPS)
            v.memset(zeros[:, :], 0.0).then_inc(ones_done, 1)
            v_.wait_ge(iota_done, 2)
            step(v.tensor_copy(row_f[:, :], row_i[:, :]))
            v.tensor_scalar(ident[:, :], few[:, :], row_f[:, 0:1], None, ALU.is_equal).then_inc(ident_done, 1)
            v.tensor_scalar(upper[:, :], few[0:HALF, :], float(HALF), row_f[0:HALF, 0:1], ALU.subtract, ALU.is_equal)
            step(v.tensor_copy(steps_f[:, :], few[:, :]))
            v.tensor_copy(steps[:, :, :], steps_f[:, 0:HALVES].unsqueeze(2).broadcast_to([P, HALVES, HOT_DVE])).then_inc(steps_done, 1)

            v_.wait_ge(dst_in, 16 * 3)
            v.tensor_copy(dst_f, raw_dst[:, :, :].rearrange("p a b -> p (a b)")).then_inc(dst_float, 1)
            for a in range(RA):
                v_.wait_ge(edge_turned, a + 1)
                v.tensor_copy(dstT[:, a * P:(a + 1) * P], ps_e[a % 2][:, 0:P]).then_inc(edge_kept, 1)
            v_.wait_ge(edge_kept, RA)
            v.tensor_scalar(lo_i, dstT[:, :], HALF - 1, None, ALU.bitwise_and).then_inc(split_i, 1)
            step(v.tensor_scalar(hi_i, dstT[:, :], HALF.bit_length() - 1, None, ALU.arith_shift_right))
            v.tensor_copy(hi[:, :], hi_i).then_inc(split_done, 1)
            v_.wait_ge(src_in, 16 * 3)
            v.tensor_scalar(place[:, :], raw_src[0:SLOTS, 0, :], P - 1, None, ALU.bitwise_and).then_inc(place_done, 1)
            v_.wait_ge(split_done, 2)
            v_.wait_ge(steps_done, 1)

            with v_.Fori(0, HSTEPS) as i:
                for b in range(2):
                    v_.wait_ge(hot_used, 2 * i + b + 1)
                    c0 = (2 * i + b) * HOT
                    v.tensor_tensor(hot_v[b][:, 0:HALF, :], steps[:, 0:HALF, :],
                                    lo[:, bass.ds(c0, HOT_DVE)].unsqueeze(1).broadcast_to([P, HALF, HOT_DVE]), ALU.is_equal)
                    v.tensor_tensor(hot_v[b][:, HALF:, :], steps[:, :, :],
                                    hi[:, bass.ds(c0, HOT_DVE)].unsqueeze(1).broadcast_to([P, HALVES, HOT_DVE]),
                                    ALU.is_equal).then_inc(hot_made_v, 1)

            v_.wait_ge(next_in, 16 * 3)
            v_.wait_ge(hot_used, 2 * HSTEPS + 1)
            v.tensor_scalar(firsts[:, :], few[:, 0:T + 1], float(P), None, ALU.mult)
            step(v.tensor_copy(ends[:, :], raw_next[:, :, P - 2]))
            step(v.tensor_tensor(before, ends[:, :].unsqueeze(1).broadcast_to([P, T + 1, RA]),
                                 firsts[:, :].unsqueeze(2).broadcast_to([P, T + 1, RA]), ALU.is_lt))
            step(v.tensor_reduce(counts[:, 0:T + 1], before, AX.X, ALU.add))
            step(v.tensor_tensor(viol, raw_dst[:, :, :].rearrange("p a b -> p (a b)"),
                                 raw_next[:, :, :].rearrange("p a b -> p (a b)"), ALU.is_gt))
            v.tensor_reduce(counts[:, T + 1:T + 2], viol, AX.X, ALU.add).then_inc(counts_in, 1)

            v_.wait_ge(deg_done, 1)
            v.tensor_scalar(deg[:, :, :], ps_d[0:HALF, 0:HALVES].rearrange("p (t h) -> p h t", h=2), 1.0, None,
                            ALU.add).then_inc(deg_done, 1)
            v_.wait_ge(root_done, 1)
            v.reciprocal(dinv[:, :], root[:, :]).then_inc(dinv_done, 1)
            v_.wait_ge(dinv_done, 1)
            v_.wait_ge(x_in, 16 * (XSTEPS + 1))
            for g in range(XSTEPS):
                if X_BY[g][0] == 0:
                    t0 = g * XG
                    v.tensor_tensor(xs[:, t0:t0 + XG, :], xs[:, t0:t0 + XG, :],
                                    dinv[:, t0:t0 + XG].unsqueeze(2).broadcast_to([P, XG, C]),
                                    ALU.mult).then_inc(x_scaled[0], 1)

            def prepare(n, t, base, part):
                if part == 0:
                    v_.wait_ge(front_used, n + 1)
                elif not isinstance(n, int) or n > 0:
                    v_.wait_ge(opened, n + 1)
                k = part * FRONT
                v.tensor_copy(idx[:, k:k + FRONT], srcT[:, bass.ds(base + k, FRONT)]).then_inc((front_idx, back_idx)[part], 1)
                v.tensor_tensor(sel[:, k:k + FRONT, :],
                                ids[:, bass.ds(t * P, P)].unsqueeze(1).broadcast_to([P, FRONT, P]),
                                dstT[:, bass.ds(base + k, FRONT)].unsqueeze(2).broadcast_to([P, FRONT, P]),
                                ALU.is_equal).then_inc((front_ready, back_ready)[part], 1)

            v.tensor_scalar(tile_i[:, :], srcT[:, 0:SLOTS], P.bit_length() - 1, None, ALU.arith_shift_right)
            step(v.memset(src_dinv[:, :], 0.0))
            step(v.tensor_tensor(in_tile, few[:, 0:T].unsqueeze(1).broadcast_to([P, SLOTS, T]),
                                 tile_i[:, :].unsqueeze(2).broadcast_to([P, SLOTS, T]), ALU.is_equal))
            v_.wait_ge(src_dinv_spread, 1)
            for part, ps in enumerate((ps_h, ps_o)):
                ks = slice(part * FRONT, part * FRONT + FRONT)
                ins = v.tensor_tensor(of_tile[:, ks, :], ps[:, 0:FRONT * T].rearrange("p (k t) -> p k t", t=T),
                                      in_tile[:, ks, :], ALU.mult)
            step(ins)
            v.tensor_reduce(src_dinv[:, :], of_tile, AX.X, ALU.add).then_inc(src_dinv_done, 1)
            v_.wait_ge(src_dinv_done, 1)
            for g, group in enumerate(GROUPS):
                if group[0] < FRONT:
                    v_.wait_ge(landed[g], 16 * len(group))
            v.tensor_tensor(rows[:, 0:FRONT, 0:C], rows[:, 0:FRONT, 0:C],
                            src_dinv[:, 0:FRONT].unsqueeze(2).broadcast_to([P, FRONT, C]), ALU.mult).then_inc(front_scaled, 1)
            v_.wait_ge(iota_done, 3)
            v_.wait_ge(src_kept, RA)
            v_.wait_ge(hot_used, 2 * HSTEPS + 2)
            prepare(0, 0, 0, 0)
            prepare(0, 0, 0, 1)

            v_.wait_ge(counts_done, 1)
            step(v.tensor_copy(ctl[:, :], ps_T[0:1, 0:T + 2]))
            step(v.tensor_tensor(moved[:, :], ctl[:, 1:T + 1], ctl[:, 0:T], ALU.subtract))
            v.tensor_scalar(odd[:, 0, :], moved[:, :], float(FRONT), None, ALU.is_lt)
            step(v.tensor_scalar(odd[:, 1, :], moved[:, :], float(SLOTS - 1), None, ALU.is_gt))
            step(v.tensor_reduce(bad[:, 0:1], odd[:, :, :].rearrange("p a b -> p (a b)"), AX.X, ALU.add))
            step(v.tensor_tensor(bad[:, 1:2], bad[:, 0:1], ctl[:, T + 1:T + 2], ALU.add))
            step(v.tensor_scalar(bad[:, 2:3], bad[:, 1:2], 0.0, None, ALU.is_gt))
            v.tensor_copy(general_i[:, :], bad[:, 2:3])
            v.tensor_copy(base_i[:, :], ctl[:, 0:T + 1])
            v.tensor_copy(need_i[:, 1:T], moved[:, 1:T])
            v.memset(need_i[:, 0:1], 99)
            v.tensor_copy(slot0_i[:, 1:T + 1], moved[:, :])
            v.memset(slot0_i[:, 0:1], 0).then_inc(control_done, 1)
            v_.wait_ge(control_done, 1)

            def early_and_late():
                v.tensor_tensor(late_hot, ids[:, LATE:LATE + P].unsqueeze(1).broadcast_to([P, SLOTS, P]),
                                srcT[:, 0:SLOTS].unsqueeze(2).broadcast_to([P, SLOTS, P]), ALU.is_equal)
                v.tensor_tensor(first_hot, few[:, :].unsqueeze(1).broadcast_to([P, SLOTS, P]),
                                dstT[:, 0:SLOTS].unsqueeze(2).broadcast_to([P, SLOTS, P]), ALU.is_equal).then_inc(late_made, 1)
                v.tensor_scalar(keep[:, :], srcT[:, 0:SLOTS], LATE, None, ALU.is_lt)
                step(v.tensor_scalar(above[:, 0, :], dstT[:, 0:SLOTS], 1, None, ALU.add))
                v.tensor_tensor(early_src[:, :], srcT[:, 0:SLOTS], keep[:, :], ALU.mult)
                step(v.tensor_tensor(above[:, 1, :], above[:, 0, :], keep[:, :], ALU.mult))
                step(v.tensor_scalar(early_dst[:, :], above[:, 1, :], 1, None, ALU.subtract))

            def prepare_early(n, part):
                if part == 0:
                    v_.wait_ge(front_used, n + 1)
                else:
                    v_.wait_ge(window_done, n)
                k = part * FRONT
                v.tensor_copy(idx[:, k:k + FRONT], early_src[:, k:k + FRONT]).then_inc((front_idx, back_idx)[part], 1)
                v.tensor_tensor(sel[:, k:k + FRONT, :], few[:, :].unsqueeze(1).broadcast_to([P, FRONT, P]),
                                early_dst[:, k:k + FRONT].unsqueeze(2).broadcast_to([P, FRONT, P]),
                                ALU.is_equal).then_inc((front_ready, back_ready)[part], 1)

            def take_sum(phase, n, tile, first):
                v_.wait_ge(window_done, n + 1)
                if first:
                    v_.wait_ge(own_in, 16 * (tile + 1))
                w = WIDTH[phase]
                v.tensor_tensor(acc[:, 0:w], ps_acc[:, 0:w], acc[:, 0:w], ALU.add).then_inc(sum_taken, 1)

            def finish(t, taken):
                v_.wait_ge(sum_taken, taken)
                v.scalar_tensor_tensor(y1[:, :], acc[:, 0:C], dinv[:, bass.ds(t, 1)], b3b[:, :], ALU.mult, ALU.add).then_inc(acc_used, 1)
                v_.wait_ge(acc_used, nth(2, t) + 2)
                v_.wait_ge(res_in, 16 * (t + 1))
                v.scalar_tensor_tensor(y2[:, :], y1[:, :], 0.0, res[:, :], ALU.max, ALU.add).then_inc(y_step, 1)
                v_.wait_ge(y_step, 2 * t + 1)
                v.bn_stats(stats[:, :], y2[:, :]).then_inc(y_step, 1)
                v_.wait_ge(y_step, 2 * t + 2)
                v_.sem_inc(dve_step, 1)
                v.bn_aggr(mv[:, :], stats[:, :]).then_inc(var_ready, 1)
                v_.wait_ge(sd_ready, t + 1)
                v.reciprocal(rstd[:, :], sd[:, :]).then_inc(var_ready, 1)
                v_.wait_ge(var_ready, 2 * t + 2)
                v_.wait_ge(y3_free, t + 1)
                v.tensor_scalar(y3[:, :], y2[:, :], mv[:, 0:1], rstd[:, 0:1], ALU.subtract, ALU.mult).then_inc(y_ready, 1)

            def base_of(t):
                return v_.value_load(base_i[0:1, bass.ds(t, 1)], min_val=0, max_val=CH - 1)

            def one_window():
                def steady(phase, t):
                    n = nth(phase, t)
                    base = base_of(t)
                    prepare(n, t, base, 0)
                    take_sum(phase, n - 1, n - 1, True)
                    prepare(n, t, base, 1)
                    if phase == 2:
                        finish(t - 1, n + 1)

                for phase in range(3):
                    if phase == 0:
                        steady(phase, 1)
                        early_and_late()
                        steady(phase, 2)
                        v_.wait_ge(late_summed, 1)
                        v.tensor_copy(late[:, :], ps_l[:, 0:P])
                    with v_.Fori(3 if phase == 0 else 1, T) as t:
                        steady(phase, t)
                    n = nth(phase, T)
                    if phase < 2:
                        prepare_early(n, 0)
                    take_sum(phase, n - 1, n - 1, True)
                    if phase < 2:
                        prepare_early(n, 1)
                    if phase == 2:
                        finish(T - 1, n + 1)

            def sweeps():
                def tile_sweep(phase, t, prepared=False):
                    tile = nth(phase, t)

                    def one(w, first, prepared=False):
                        n = nth_window(phase, t, SWEEP, w)
                        if not prepared:
                            prepare(n, t, w * SLOTS, 0)
                            prepare(n, t, w * SLOTS, 1)
                        v_.wait_ge(sum_taken, n + 1)
                        take_sum(phase, n, tile, first)
                    one(0, True, prepared)
                    with v_.Fori(1, SWEEP) as w:
                        one(w, False)
                    if phase == 2:
                        finish(t, (tile + 1) * SWEEP + 1)

                tile_sweep(0, 0, True)
                for phase in range(3):
                    with v_.Fori(1 if phase == 0 else 0, T) as t:
                        tile_sweep(phase, t)

            general = v_.value_load(general_i[0:1, 0:1], min_val=0, max_val=1)
            with v_.If(general == 0):
                one_window()
            with v_.Else():
                sweeps()

        @block.scalar
        def _(act):
            act.wait_ge(src_in, 16 * 3)
            nc.scalar.activation(src_f, raw_src[:, :, :].rearrange("p a b -> p (a b)"), ACT.Copy).then_inc(src_float, 1)
            act.wait_ge(split_i, 1)
            nc.scalar.activation(lo[:, :], lo_i, ACT.Copy).then_inc(split_done, 1)
            act.wait_ge(next_in, 16 * 3)
            act.dma_start(w1[:, :, :], W1.rearrange("(k p) n -> p k n", p=P)).then_inc(weights_in, 16)
            act.dma_start(w2[:, :, :], W2.rearrange("(k p) n -> p k n", p=P)).then_inc(weights_in, 16)
            act.dma_start(w3[:, :, :], W3.rearrange("(k p) n -> p k n", p=P)).then_inc(weights_in, 16)
            act.dma_start(b3b[:, :], b3.rearrange("(a c) -> a c", a=1).broadcast_to([P, C])).then_inc(weights_in, 16)
            with nc.allow_non_contiguous_dma(reason="two bias vectors, one value to a partition"):
                act.dma_start(b1T[:, :], b1.rearrange("(m p) -> p m", p=P)).then_inc(weights_in, 16)
                act.dma_start(b2T[:, :], b2.rearrange("(m p) -> p m", p=P)).then_inc(weights_in, 16)

            act.wait_ge(src_turned, 1)
            nc.scalar.activation(srcT[:, 0:P], ps_e[0][:, 0:P], ACT.Copy).then_inc(src_kept, 1)
            act.wait_ge(split_done, 2)
            act.wait_ge(steps_done, 1)
            with act.Fori(0, HSTEPS) as i:
                for b in range(2):
                    act.wait_ge(hot_used, 2 * i + b + 1)
                    act.sem_inc(act_step, 1)
                    c0 = (2 * i + b) * HOT + HOT_DVE
                    for c in range(HOT_ACT):
                        nc.scalar.activation(away[:, b, c, 0:HALF], steps_f[:, 0:HALF], ACT.Abs, bias=lo[:, bass.ds(c0 + c, 1)], scale=-1.0)
                        last = nc.scalar.activation(away[:, b, c, HALF:], steps_f[:, 0:HALVES], ACT.Abs,
                                                    bias=hi[:, bass.ds(c0 + c, 1)], scale=-1.0)
                    last.then_inc(away_done, 1)
                    act.wait_ge(away_done, 2 * i + b + 1)
                    nc.scalar.activation(hot_a[b][:, :, :], away[:, b, :, :], ACT.Relu, bias=ones[:, 0:1],
                                         scale=-1.0).then_inc(hot_made_a, 1)
            act.wait_ge(deg_done, 3)
            nc.scalar.activation(root[:, :], ps_l[:, 0:T], ACT.Sqrt).then_inc(root_done, 1)
            act.wait_ge(dinv_done, 1)
            act.wait_ge(x_in, 16 * (XSTEPS + 1))
            for g in range(XSTEPS):
                if X_BY[g][0] == 1:
                    for t in range(g * XG, (g + 1) * XG):
                        ins = nc.scalar.activation(xs[:, t, :], xs[:, t, :], ACT.Copy, scale=dinv[:, t:t + 1])
                    ins.then_inc(x_scaled[1], 1)
            for a in range(1, RA):
                act.wait_ge(src_turned, a + 1)
                nc.scalar.activation(srcT[:, a * P:(a + 1) * P], ps_e[a % 2][:, 0:P], ACT.Copy).then_inc(src_kept, 1)
            act.wait_ge(src_dinv_done, 1)
            for k in range(FRONT, SLOTS):
                for g, group in enumerate(GROUPS):
                    if k == group[0]:
                        act.wait_ge(landed[g], 16 * len(group))
                ins = nc.scalar.activation(rows[:, k, 0:C], rows[:, k, 0:C], ACT.Copy, scale=src_dinv[:, k:k + 1])
            ins.then_inc(back_scaled, 1)
            act.sem_inc(acc_used, 1)
            act.wait_ge(weights_in, 16 * 6)

            def scale(phase, t, per):
                n = nth(phase, t)
                w = WIDTH[phase]
                act.wait_ge(sum_taken, (n + 1) * per + 1)
                act.sem_inc(act_step, 1)
                nc.scalar.activation(agg[:, 0:w], acc[:, 0:w], ACT.Copy, scale=dinv[:, bass.ds(t, 1)]).then_inc(agg_ready, 1)
                act.wait_ge(agg_ready, n + 1)
                act.sem_inc(acc_used, 1)

            def relu_T(ps, bias, m):
                nc.scalar.activation(hT[:, m * P:(m + 1) * P], ps, ACT.Relu,
                                     bias=bias[:, m:m + 1]).then_inc(hT_ready, 1)

            def tile(phase, t, per):
                n = nth(phase, t)
                scale(phase, t, per)
                if phase == 0:
                    act.wait_ge(turned, n + 1)
                    nc.scalar.activation(aggT[:, 0:C], ps_T[:, 0:C], ACT.Copy).then_inc(aggT_ready, 1)
                    for m in range(KH):
                        act.wait_ge(h_done, KH * t + m + 1)
                        relu_T(hidden_banks[m], b1T, m)
                else:
                    act.wait_ge(turned, n + 1)
                    for m in range(KH):
                        relu_T(ps_T[:, m * P:(m + 1) * P], b2T, m)
                w = WIDTH[phase + 1]
                act.wait_ge(o_done, n + 1)
                act.wait_ge(made_free, n + 1)
                act.sem_inc(act_step, 1)
                nc.scalar.activation(made[:, 0:w], ps_o[:, 0:w], ACT.Copy, scale=dinv[:, bass.ds(t, 1)]).then_inc(made_ready, 1)

            def deviation(t):
                act.wait_ge(var_ready, 2 * t + 1)
                nc.scalar.activation(sd[:, :], mv[:, 1:2], ACT.Sqrt, bias=eps[:, 0:1]).then_inc(sd_ready, 1)

            def phases(per):
                for phase in range(2):
                    with act.Fori(0, T) as t:
                        tile(phase, t, per)
                with act.Fori(0, T) as t:
                    deviation(t)

            act.wait_ge(control_done, 1)
            general = act.value_load(general_i[0:1, 0:1], min_val=0, max_val=1)
            with act.If(general == 0):
                phases(1)
            with act.Else():
                phases(SWEEP)

        @block.tensor
        def _(pe):
            mm = nc.tensor.matmul
            pe.sem_inc(hot_used, 2)
            pe.sem_inc(front_used, 1)
            pe.sem_inc(sum_taken, 1)
            pe.wait_ge(ident_done, 1)

            def turn_edges(of, floated, turned_, kept, blocks):
                pe.wait_ge(floated, 1)
                for a in blocks:
                    if a >= 2:
                        pe.wait_ge(kept, a - 1)
                    nc.tensor.transpose(ps_e[a % 2][:, 0:P], of[:, a * P:(a + 1) * P], ident[:, :]).then_inc(turned_, 1)

            turn_edges(dst_f, dst_float, edge_turned, edge_kept, range(RA))
            pe.wait_ge(edge_kept, RA)
            turn_edges(src_f, src_float, src_turned, src_kept, range(1))
            pe.wait_ge(ones_done, 1)
            mm(ps_d[0:HALF, 0:HALVES], zeros[:, 0:HALF], zeros[:, 0:HALVES], start=True, stop=False, skip_group_check=True)
            with pe.Fori(0, HSTEPS) as i:
                for b in range(2):
                    n = 2 * i + b + 1

                    def add(place, tile):
                        return mm(ps_d[0:HALF, 0:HALVES], place, tile, start=False, stop=False, skip_group_check=True)

                    pe.wait_ge(hot_made_v, n)
                    for c in range(HOT_DVE):
                        add(hot_v[b][:, 0:HALF, c], hot_v[b][:, HALF:, c])
                    pe.wait_ge(hot_made_a, n)
                    for c in range(HOT_ACT):
                        last = add(hot_a[b][:, c, 0:HALF], hot_a[b][:, c, HALF:])
                    last.then_inc(hot_used, 1)
            mm(ps_d[0:HALF, 0:HALVES], zeros[:, 0:HALF], zeros[:, 0:HALVES], start=False, stop=True,
               skip_group_check=True).then_inc(deg_done, 1)
            pe.wait_ge(deg_done, 2)
            mm(ps_l[:, 0:T], ident[0:HALF, :], deg[:, 0, :], start=True, stop=False)
            mm(ps_l[:, 0:T], upper[:, :], deg[:, 1, :], start=False, stop=True).then_inc(deg_done, 1)
            pe.wait_ge(here_done, 1)
            pe.wait_ge(dinv_done, 1)
            for k in range(SLOTS):
                ins = mm((ps_h, ps_o)[k // FRONT][:, k % FRONT * T:(k % FRONT + 1) * T], is_here[:, k, :], dinv[:, :],
                         start=True, stop=True)
            ins.then_inc(src_dinv_spread, 1)
            turn_edges(src_f, src_float, src_turned, src_kept, range(1, RA))
            pe.wait_ge(counts_in, 1)
            mm(ps_T[:, 0:T + 2], ones[:, :], counts[:, :], start=True, stop=True).then_inc(counts_done, 1)
            def slots(phase, n, ks, first, need=None):
                w = WIDTH[phase]
                for k in ks:
                    for g, s in enumerate(GROUPS):
                        if k == next(o for o in ORDER if o in s):
                            pe.wait_ge(landed[g], 16 * len(s) * (n + 1))
                    if k == 0:
                        pe.wait_ge(front_ready, n + 1)
                        pe.wait_ge(sum_taken, n + 1)
                    if k == FRONT:
                        pe.wait_ge(back_ready, n + 1)
                    if need is not None and k >= SURE:
                        with pe.If(need >= k):
                            mm(ps_acc[:, 0:w], sel[:, k, :], rows[:, k, 0:w], start=False, stop=False)
                        continue
                    ins = mm(ps_acc[:, 0:w], sel[:, k, :], first if k == 0 else rows[:, k, 0:w],
                             start=(k == 0), stop=(k == ORDER[-1]))
                    if k == 0:
                        ins.then_inc(opened, 1)
                    if k == FRONT - 1:
                        ins.then_inc(front_used, 1)
                    if k == ORDER[-1]:
                        ins.then_inc(window_done, 1)

            def turn(phase, t):
                n = nth(phase, t)
                pe.wait_ge(agg_ready, n + 1)
                for m in range(WIDTH[phase] // P):
                    ins = nc.tensor.transpose(ps_T[:, m * P:(m + 1) * P], agg[:, m * P:(m + 1) * P], ident[:, :])
                ins.then_inc(turned, 1)

            def hidden(t):
                pe.wait_ge(aggT_ready, t + 1)
                for m in range(KH):
                    for k in range(KC):
                        ins = mm(hidden_banks[m], w1[:, k, m * P:(m + 1) * P], aggT[:, k * P:(k + 1) * P],
                                 start=(k == 0), stop=(k == KC - 1))
                    ins.then_inc(h_done, 1)

            def product(phase, t):
                n = nth(phase, t)
                w = WIDTH[phase + 1]
                wt = w2 if phase == 0 else w3
                for m in range(KH):
                    pe.wait_ge(hT_ready, KH * n + m + 1)
                    ins = mm(ps_o[:, 0:w], hT[:, m * P:(m + 1) * P], wt[:, m, :], start=(m == 0), stop=(m == KH - 1))
                ins.then_inc(o_done, 1)

            def one_window():
                for phase in range(3):
                    def first_rows(t):
                        at = pe.value_load(slot0_i[0:1, bass.ds(t, 1)], min_val=0, max_val=SLOTS - 1)
                        return rows[:, bass.ds(at, 1), 0:WIDTH[phase]].rearrange("p a w -> p (a w)")

                    def steady(t, places):
                        n = nth(phase, t)
                        need = pe.value_load(need_i[0:1, bass.ds(t, 1)], min_val=0, max_val=99)
                        at_turn, at_hidden, at_product = places
                        slots(phase, n, ORDER[0:at_turn], first_rows(t))
                        if phase < 2:
                            turn(phase, t - 1)
                        slots(phase, n, ORDER[at_turn:at_hidden], None, need)
                        if phase == 0:
                            hidden(t - 1)
                        slots(phase, n, ORDER[at_hidden:at_product], None, need)
                        if phase < 2:
                            product(phase, t - 1)
                        slots(phase, n, ORDER[at_product:], None, need)

                    if phase > 0:
                        n = nth(phase, 0)
                        slots(phase, n, ORDER[:-1], rows[:, 0, 0:WIDTH[phase]])
                        pe.wait_ge(made_ready, n)
                        mm(ps_acc[:, 0:WIDTH[phase]], late[:, :], made[:, 0:WIDTH[phase]], start=False, stop=False)
                        slots(phase, n, ORDER[-1:], None)
                    if phase == 0:
                        steady(1, (5, 9, 12))
                        pe.wait_ge(late_made, 1)
                        for k in range(SLOTS):
                            ins = mm(ps_l[:, 0:P], late_hot[:, k, :], first_hot[:, k, :], start=(k == 0), stop=(k == SLOTS - 1))
                        ins.then_inc(late_summed, 1)
                        steady(2, (5, 9, 12))
                    with pe.Fori(3 if phase == 0 else 1, T - 1) as t:
                        steady(t, (5, 9, SLOTS if phase == 1 else 12))
                    steady(T - 1, LAST_PLACES[phase])
                    if phase < 2:
                        turn(phase, T - 1)
                        if phase == 0:
                            hidden(T - 1)
                        product(phase, T - 1)

            def sweeps():
                def rest(phase, t, w0):
                    with pe.Fori(w0, SWEEP) as w:
                        slots(phase, nth_window(phase, t, SWEEP, w), ORDER, rows[:, 0, 0:WIDTH[phase]])
                    if phase < 2:
                        turn(phase, t)
                        if phase == 0:
                            hidden(t)
                        product(phase, t)

                rest(0, 0, 1)
                for phase in range(3):
                    with pe.Fori(1 if phase == 0 else 0, T) as t:
                        rest(phase, t, 0)

            pe.wait_ge(front_scaled, 1)
            pe.wait_ge(back_scaled, 1)
            slots(0, 0, ORDER, rows[:, 0, 0:C])
            pe.wait_ge(control_done, 1)
            pe.wait_ge(weights_in, 16 * 6)
            general = pe.value_load(general_i[0:1, 0:1], min_val=0, max_val=1)
            with pe.If(general == 0):
                one_window()
            with pe.Else():
                sweeps()


_INS = ['x', 'src', 'dst', 'L0_gnn_W1', 'L0_gnn_b1', 'L0_gnn_W2', 'L0_gnn_b2', 'L0_gnn_W3', 'L0_gnn_b3']


def kernel(**inputs):
    import numpy as _np
    import concourse.bacc as _bacc
    from concourse import mybir as _mybir
    from concourse.bass_utils import run_bass_kernel_spmd as _run

    nc = _bacc.Bacc("TRN2", target_bir_lowering=False, num_devices=1)
    arrays, args = {}, []
    for name in _INS:
        a = _np.ascontiguousarray(inputs[name])
        arrays[f"in_{name}_dram"] = a
        args.append(nc.dram_tensor(f"in_{name}_dram", a.shape, _mybir.dt.from_np(a.dtype), kind="ExternalInput").ap())
    out = nc.dram_tensor("out_0_dram", inputs["x"].shape, _mybir.dt.float32, kind="ExternalOutput").ap()
    gnn_program(nc, *args, out)
    r = _run(nc, [arrays], core_ids=[0])
    return r.results[0]["out_0_dram"]
```
